# Optimizing a Trainium2 kernel written in Bass

```python
import numpy as np
import jax
import jax.numpy as jnp

def _softmax(x, axis=-1):
    return jax.nn.softmax(x, axis=axis)

def _gelu(x):
    return jax.nn.gelu(x, approximate=True)

def _silu(x):
    return jax.nn.silu(x)

def _sigmoid(x):
    return jax.nn.sigmoid(x)

def _layernorm(x, axis=-1, eps=1e-05):
    m = jnp.mean(x, axis=axis, keepdims=True)
    v = jnp.var(x, axis=axis, keepdims=True)
    return (x - m) / jnp.sqrt(v + eps)

def _scatter_add(tgt, idx, src, axis=0):
    return tgt.at[idx].add(src)

def _segment_sum(src, seg, n):
    return jax.ops.segment_sum(src, seg, n)
kernel_name = 'mk_dlrm_tower_d1_rec_r8_7601f8'

def setup_inputs(seed: int=0):
    np.random.seed(seed)
    _w = jnp.asarray

    def _rec_inputs():
        import jax
        import jax.numpy as jnp
        _tk = jax.random.key(seed)
        dense_ctx = jax.random.normal(jax.random.fold_in(_tk, 190), (1024, 16), jnp.float32)
        ids = jnp.stack([jax.random.randint(jax.random.fold_in(_tk, 200 + f), (1024,), 0, v, jnp.int32) for f, v in enumerate([12500, 12500, 125000, 125000, 125000, 1000, 1250, 12500, 1000, 125000, 1250, 12500, 1250, 12500, 125000, 12500, 125000, 1000, 125000, 1250, 125000, 1000, 12500, 125000, 12500, 1000, 12500, 1000, 1250, 12500, 12500, 1000, 1250, 1250, 125000, 1250, 125000, 1250, 125000])], axis=1)
        tbl_0 = 0.05 * jax.random.normal(jax.random.fold_in(_tk, 500 + 0), (12500, 16), jnp.float32)
        tbl_1 = 0.05 * jax.random.normal(jax.random.fold_in(_tk, 500 + 1), (12500, 16), jnp.float32)
        tbl_2 = 0.05 * jax.random.normal(jax.random.fold_in(_tk, 500 + 2), (125000, 16), jnp.float32)
        tbl_3 = 0.05 * jax.random.normal(jax.random.fold_in(_tk, 500 + 3), (125000, 16), jnp.float32)
        tbl_4 = 0.05 * jax.random.normal(jax.random.fold_in(_tk, 500 + 4), (125000, 16), jnp.float32)
        tbl_5 = 0.05 * jax.random.normal(jax.random.fold_in(_tk, 500 + 5), (1000, 16), jnp.float32)
        tbl_6 = 0.05 * jax.random.normal(jax.random.fold_in(_tk, 500 + 6), (1250, 16), jnp.float32)
        tbl_7 = 0.05 * jax.random.normal(jax.random.fold_in(_tk, 500 + 7), (12500, 16), jnp.float32)
        tbl_8 = 0.05 * jax.random.normal(jax.random.fold_in(_tk, 500 + 8), (1000, 16), jnp.float32)
        tbl_9 = 0.05 * jax.random.normal(jax.random.fold_in(_tk, 500 + 9), (125000, 16), jnp.float32)
        tbl_10 = 0.05 * jax.random.normal(jax.random.fold_in(_tk, 500 + 10), (1250, 16), jnp.float32)
        tbl_11 = 0.05 * jax.random.normal(jax.random.fold_in(_tk, 500 + 11), (12500, 16), jnp.float32)
        tbl_12 = 0.05 * jax.random.normal(jax.random.fold_in(_tk, 500 + 12), (1250, 16), jnp.float32)
        tbl_13 = 0.05 * jax.random.normal(jax.random.fold_in(_tk, 500 + 13), (12500, 16), jnp.float32)
        tbl_14 = 0.05 * jax.random.normal(jax.random.fold_in(_tk, 500 + 14), (125000, 16), jnp.float32)
        tbl_15 = 0.05 * jax.random.normal(jax.random.fold_in(_tk, 500 + 15), (12500, 16), jnp.float32)
        tbl_16 = 0.05 * jax.random.normal(jax.random.fold_in(_tk, 500 + 16), (125000, 16), jnp.float32)
        tbl_17 = 0.05 * jax.random.normal(jax.random.fold_in(_tk, 500 + 17), (1000, 16), jnp.float32)
        tbl_18 = 0.05 * jax.random.normal(jax.random.fold_in(_tk, 500 + 18), (125000, 16), jnp.float32)
        tbl_19 = 0.05 * jax.random.normal(jax.random.fold_in(_tk, 500 + 19), (1250, 16), jnp.float32)
        tbl_20 = 0.05 * jax.random.normal(jax.random.fold_in(_tk, 500 + 20), (125000, 16), jnp.float32)
        tbl_21 = 0.05 * jax.random.normal(jax.random.fold_in(_tk, 500 + 21), (1000, 16), jnp.float32)
        tbl_22 = 0.05 * jax.random.normal(jax.random.fold_in(_tk, 500 + 22), (12500, 16), jnp.float32)
        tbl_23 = 0.05 * jax.random.normal(jax.random.fold_in(_tk, 500 + 23), (125000, 16), jnp.float32)
        tbl_24 = 0.05 * jax.random.normal(jax.random.fold_in(_tk, 500 + 24), (12500, 16), jnp.float32)
        tbl_25 = 0.05 * jax.random.normal(jax.random.fold_in(_tk, 500 + 25), (1000, 16), jnp.float32)
        tbl_26 = 0.05 * jax.random.normal(jax.random.fold_in(_tk, 500 + 26), (12500, 16), jnp.float32)
        tbl_27 = 0.05 * jax.random.normal(jax.random.fold_in(_tk, 500 + 27), (1000, 16), jnp.float32)
        tbl_28 = 0.05 * jax.random.normal(jax.random.fold_in(_tk, 500 + 28), (1250, 16), jnp.float32)
        tbl_29 = 0.05 * jax.random.normal(jax.random.fold_in(_tk, 500 + 29), (12500, 16), jnp.float32)
        tbl_30 = 0.05 * jax.random.normal(jax.random.fold_in(_tk, 500 + 30), (12500, 16), jnp.float32)
        tbl_31 = 0.05 * jax.random.normal(jax.random.fold_in(_tk, 500 + 31), (1000, 16), jnp.float32)
        tbl_32 = 0.05 * jax.random.normal(jax.random.fold_in(_tk, 500 + 32), (1250, 16), jnp.float32)
        tbl_33 = 0.05 * jax.random.normal(jax.random.fold_in(_tk, 500 + 33), (1250, 16), jnp.float32)
        tbl_34 = 0.05 * jax.random.normal(jax.random.fold_in(_tk, 500 + 34), (125000, 16), jnp.float32)
        tbl_35 = 0.05 * jax.random.normal(jax.random.fold_in(_tk, 500 + 35), (1250, 16), jnp.float32)
        tbl_36 = 0.05 * jax.random.normal(jax.random.fold_in(_tk, 500 + 36), (125000, 16), jnp.float32)
        tbl_37 = 0.05 * jax.random.normal(jax.random.fold_in(_tk, 500 + 37), (1250, 16), jnp.float32)
        tbl_38 = 0.05 * jax.random.normal(jax.random.fold_in(_tk, 500 + 38), (125000, 16), jnp.float32)
        _rk = jax.random.fold_in(_tk, 7)
        W_top1 = 0.0693375 * jax.random.normal(jax.random.fold_in(_tk, 801), (208, 512), jnp.float32)
        W_top2 = 0.0441942 * jax.random.normal(jax.random.fold_in(_tk, 802), (512, 256), jnp.float32)
        W_top3 = 0.0625 * jax.random.normal(jax.random.fold_in(_tk, 803), (256, 1), jnp.float32)
        b_top1 = jnp.zeros((512,), jnp.float32)
        b_top2 = jnp.zeros((256,), jnp.float32)
        return (dense_ctx, ids, tbl_0, tbl_1, tbl_2, tbl_3, tbl_4, tbl_5, tbl_6, tbl_7, tbl_8, tbl_9, tbl_10, tbl_11, tbl_12, tbl_13, tbl_14, tbl_15, tbl_16, tbl_17, tbl_18, tbl_19, tbl_20, tbl_21, tbl_22, tbl_23, tbl_24, tbl_25, tbl_26, tbl_27, tbl_28, tbl_29, tbl_30, tbl_31, tbl_32, tbl_33, tbl_34, tbl_35, tbl_36, tbl_37, tbl_38, W_top1, b_top1, W_top2, b_top2, W_top3)
    dense_ctx, ids, tbl_0, tbl_1, tbl_2, tbl_3, tbl_4, tbl_5, tbl_6, tbl_7, tbl_8, tbl_9, tbl_10, tbl_11, tbl_12, tbl_13, tbl_14, tbl_15, tbl_16, tbl_17, tbl_18, tbl_19, tbl_20, tbl_21, tbl_22, tbl_23, tbl_24, tbl_25, tbl_26, tbl_27, tbl_28, tbl_29, tbl_30, tbl_31, tbl_32, tbl_33, tbl_34, tbl_35, tbl_36, tbl_37, tbl_38, W_top1, b_top1, W_top2, b_top2, W_top3 = _rec_inputs()

    def _L0_rec_setup():
        import jax, jax.numpy as jnp
        import numpy as np
        key = jax.random.key(seed)
        k1, k2, k3 = jax.random.split(key, 3)
        B, F0, D = (1024, 39, 16)
        L = 128
        hash_x = jax.random.normal(k1, (B, F0, D), dtype=jnp.float32)
        W0 = jax.random.normal(k2, (F0 * F0, L), dtype=jnp.float32) * 0.05
        W1 = jax.random.normal(k3, (F0 * (L // 2), L), dtype=jnp.float32) * 0.05
        return {'hash_x': hash_x, 'W0': W0, 'W1': W1}
    _L0_rec_all = _L0_rec_setup()
    _L0_rec_in = {k: v for k, v in _L0_rec_all.items() if k in ('W0', 'W1')}
    del _L0_rec_all
    return {'dense_ctx': dense_ctx, 'ids': ids, 'tbl_0': tbl_0, 'tbl_1': tbl_1, 'tbl_2': tbl_2, 'tbl_3': tbl_3, 'tbl_4': tbl_4, 'tbl_5': tbl_5, 'tbl_6': tbl_6, 'tbl_7': tbl_7, 'tbl_8': tbl_8, 'tbl_9': tbl_9, 'tbl_10': tbl_10, 'tbl_11': tbl_11, 'tbl_12': tbl_12, 'tbl_13': tbl_13, 'tbl_14': tbl_14, 'tbl_15': tbl_15, 'tbl_16': tbl_16, 'tbl_17': tbl_17, 'tbl_18': tbl_18, 'tbl_19': tbl_19, 'tbl_20': tbl_20, 'tbl_21': tbl_21, 'tbl_22': tbl_22, 'tbl_23': tbl_23, 'tbl_24': tbl_24, 'tbl_25': tbl_25, 'tbl_26': tbl_26, 'tbl_27': tbl_27, 'tbl_28': tbl_28, 'tbl_29': tbl_29, 'tbl_30': tbl_30, 'tbl_31': tbl_31, 'tbl_32': tbl_32, 'tbl_33': tbl_33, 'tbl_34': tbl_34, 'tbl_35': tbl_35, 'tbl_36': tbl_36, 'tbl_37': tbl_37, 'tbl_38': tbl_38, 'W_top1': W_top1, 'b_top1': b_top1, 'W_top2': W_top2, 'b_top2': b_top2, 'W_top3': W_top3, 'L0_rec_W0': _L0_rec_in['W0'], 'L0_rec_W1': _L0_rec_in['W1']}

def reference(dense_ctx, ids, tbl_0, tbl_1, tbl_2, tbl_3, tbl_4, tbl_5, tbl_6, tbl_7, tbl_8, tbl_9, tbl_10, tbl_11, tbl_12, tbl_13, tbl_14, tbl_15, tbl_16, tbl_17, tbl_18, tbl_19, tbl_20, tbl_21, tbl_22, tbl_23, tbl_24, tbl_25, tbl_26, tbl_27, tbl_28, tbl_29, tbl_30, tbl_31, tbl_32, tbl_33, tbl_34, tbl_35, tbl_36, tbl_37, tbl_38, W_top1, b_top1, W_top2, b_top2, W_top3, L0_rec_W0, L0_rec_W1):
    import jax
    import jax.numpy as jnp

    def _L0_rec_ref(hash_x, W0, W1):
        import jax, jax.numpy as jnp
        import numpy as np
        x0 = hash_x
        B, F0, D = x0.shape
        L = W0.shape[1]
        z0 = jnp.einsum('bid,bjd->bdij', x0, x0).reshape(B, D, F0 * F0)
        cur0 = jax.nn.relu(jnp.einsum('bdk,kl->bld', z0, W0))
        next_h, direct0 = jnp.split(cur0, 2, axis=1)
        Fk = next_h.shape[1]
        z1 = jnp.einsum('bid,bjd->bdij', x0, next_h).reshape(B, D, F0 * Fk)
        cur1 = jax.nn.relu(jnp.einsum('bdk,kl->bld', z1, W1))
        result = jnp.concatenate([direct0, cur1], axis=1)
        return jnp.sum(result, axis=-1)
    e = jnp.stack([tbl_0[ids[:, 0]], tbl_1[ids[:, 1]], tbl_2[ids[:, 2]], tbl_3[ids[:, 3]], tbl_4[ids[:, 4]], tbl_5[ids[:, 5]], tbl_6[ids[:, 6]], tbl_7[ids[:, 7]], tbl_8[ids[:, 8]], tbl_9[ids[:, 9]], tbl_10[ids[:, 10]], tbl_11[ids[:, 11]], tbl_12[ids[:, 12]], tbl_13[ids[:, 13]], tbl_14[ids[:, 14]], tbl_15[ids[:, 15]], tbl_16[ids[:, 16]], tbl_17[ids[:, 17]], tbl_18[ids[:, 18]], tbl_19[ids[:, 19]], tbl_20[ids[:, 20]], tbl_21[ids[:, 21]], tbl_22[ids[:, 22]], tbl_23[ids[:, 23]], tbl_24[ids[:, 24]], tbl_25[ids[:, 25]], tbl_26[ids[:, 26]], tbl_27[ids[:, 27]], tbl_28[ids[:, 28]], tbl_29[ids[:, 29]], tbl_30[ids[:, 30]], tbl_31[ids[:, 31]], tbl_32[ids[:, 32]], tbl_33[ids[:, 33]], tbl_34[ids[:, 34]], tbl_35[ids[:, 35]], tbl_36[ids[:, 36]], tbl_37[ids[:, 37]], tbl_38[ids[:, 38]]], axis=1)
    z = _L0_rec_ref(e, L0_rec_W0, L0_rec_W1)
    z = z.reshape(z.shape[0], -1)
    h = jnp.concatenate([z, dense_ctx], axis=1)
    h = jnp.maximum(h @ W_top1 + b_top1, 0.0)
    h = jnp.maximum(h @ W_top2 + b_top2, 0.0)
    y = h @ W_top3
    return y

_drawn_inputs = setup_inputs


def setup_inputs(seed=0):
    import zlib

    import numpy as np

    out = dict(_drawn_inputs(seed))
    spreads = {'b_top1': (0.0, 0.8), 'b_top2': (0.0, 0.443)}
    factors = {'tbl_0': 8.0,
     'tbl_1': 8.0,
     'tbl_2': 8.0,
     'tbl_3': 8.0,
     'tbl_4': 8.0,
     'tbl_5': 8.0,
     'tbl_6': 8.0,
     'tbl_7': 8.0,
     'tbl_8': 8.0,
     'tbl_9': 8.0,
     'tbl_10': 8.0,
     'tbl_11': 8.0,
     'tbl_12': 8.0,
     'tbl_13': 8.0,
     'tbl_14': 8.0,
     'tbl_15': 8.0,
     'tbl_16': 8.0,
     'tbl_17': 8.0,
     'tbl_18': 8.0,
     'tbl_19': 8.0,
     'tbl_20': 8.0,
     'tbl_21': 8.0,
     'tbl_22': 8.0,
     'tbl_23': 8.0,
     'tbl_24': 8.0,
     'tbl_25': 8.0,
     'tbl_26': 8.0,
     'tbl_27': 8.0,
     'tbl_28': 8.0,
     'tbl_29': 8.0,
     'tbl_30': 8.0,
     'tbl_31': 8.0,
     'tbl_32': 8.0,
     'tbl_33': 8.0,
     'tbl_34': 8.0,
     'tbl_35': 8.0,
     'tbl_36': 8.0,
     'tbl_37': 8.0,
     'tbl_38': 8.0,
     'L0_rec_W1': 8.0}
    for name, (base, spread) in spreads.items():
        noise = np.random.default_rng([zlib.crc32(name.encode()), seed]).standard_normal(out[name].shape)
        drawn = base * np.exp(spread * noise) if base else spread * noise
        out[name] = jnp.asarray(drawn.astype(out[name].dtype))
    for name, factor in factors.items():
        out[name] = (out[name] * factor).astype(out[name].dtype)
    return out
```

```python
from contextlib import ExitStack

import numpy as np
import concourse.bass as bass
from concourse import mybir

FIELDS, DIM, BATCH = 39, 16, 1024
HALF, WIDE = 64, 128
DENSE, TOP1, TOP2 = 16, 512, 256
P = 128
BATCHES = BATCH // P
COLS = P * DIM
U = 512
UNITS = COLS // U
DPU = U // P
N = BATCH * DIM
CYC, SHIFTS = 3, 7
PAIR0 = FIELDS * CYC
COPY_ROWS = CYC * SHIFTS - 1
GI, SI = 8, 5
GJ, TJ = 16, 4
PLAIN = 2
SPLIT = TJ - PLAIN
DIRECT_DENSE = HALF + DENSE


def tower(nc, tables, ids, w0_ij, w0_ji, w1, dense_t, w_top1, b_top1, w_top2, b_top2, w_top3,
          identity, out):
    f32, f32r, i32 = mybir.dt.float32, mybir.dt.float32r, mybir.dt.int32
    ALU, ACT, AX = mybir.AluOpType, mybir.ActivationFunctionType, mybir.AxisListType

    xt_dram = nc.dram_tensor("xt_dram", (FIELDS + COPY_ROWS, N), f32, kind="Internal").ap()
    h_dram = nc.dram_tensor("h_dram", (HALF, N), f32, kind="Internal").ap()

    with ExitStack() as ctx:
        def sb(name, shape, dtype=f32):
            return ctx.enter_context(nc.sbuf_tensor(name, shape, dtype))

        def ps(name, shape):
            return ctx.enter_context(nc.psum_tensor(name, shape, f32))

        def sem(name):
            return ctx.enter_context(nc.semaphore(name))

        w0_sb = sb("w0_sb", [PAIR0, SHIFTS, WIDE])
        w1_sb = sb("w1_sb", [P, TJ, SI, WIDE])
        w1_hi = sb("w1_hi", [P, SPLIT, SI, WIDE], f32r)
        w1_lo = sb("w1_lo", [P, SPLIT, SI, WIDE], f32r)
        wt1_sb = sb("wt1_sb", [P, 2, TOP1])
        wt2_sb = sb("wt2_sb", [P, TOP1 // P, TOP2])
        wt3_sb = sb("wt3_sb", [P, TOP2 // P])
        bt1_sb = sb("bt1_sb", [P, TOP1 // P])
        bt2_sb = sb("bt2_sb", [P, TOP2 // P])
        ident = sb("ident", [P, P])
        ids_sb = sb("ids_sb", [P, BATCHES, FIELDS], i32)
        idx = sb("idx", [P, FIELDS], i32)
        emb = sb("emb", [P, FIELDS, DIM])
        xt = sb("xt", [2 * FIELDS, 2, U])
        base = sb("base", [PAIR0, U])
        shifted = sb("shifted", [PAIR0, SHIFTS, U])
        feat_rep = [sb(f"feat_rep{k}", [P, SI, U]) for k in range(2)]
        hid_rep = [sb(f"hid_rep{k}", [P, TJ, U]) for k in range(2)]
        z0 = sb("z0", [PAIR0, SHIFTS, U])
        zp = [sb(f"zp{k}", [P, SI, U]) for k in range(PLAIN)]
        zs = [sb(f"zs{k}", [P, SI, U]) for k in range(SPLIT)]
        z_hi = [sb(f"z_hi{k}", [P, SI, U], f32r) for k in range(SPLIT)]
        z_lo = [sb(f"z_lo{k}", [P, SI, U], f32r) for k in range(SPLIT)]
        hidden = [sb(f"hidden{k}", [P, U]) for k in range(2)]
        sum0 = sb("sum0", [HALF, U])
        sum1 = sb("sum1", [P, U])
        top0 = sb("top0", [DIRECT_DENSE, BATCH])
        top1 = sb("top1", [P, BATCH])
        w0_back = z0
        act1 = [zp[k][:, 0:TOP1 // P, :] for k in range(2)]
        y_sb = [hidden[k][0:1, :] for k in range(2)]
        act2 = [zs[k][:, 0:TOP2 // P, :] for k in range(2)]

        cur0 = [ps(f"cur0_{k}", [P, U]) for k in range(2)]
        cur1 = [ps(f"cur1_{k}", [P, U]) for k in range(2)]
        xt_ps = [ps(f"xt_ps{k}", [P, U]) for k in range(2)]
        mlp_ps = [ps(f"mlp_ps{k}", [P, U]) for k in range(2)]

        w0_in = sem("w0_in")
        w1_in = sem("w1_in")
        mlp_in = sem("mlp_in")
        w0_folded = sem("w0_folded")
        w1_rounded = sem("w1_rounded")
        w1_split = sem("w1_split")
        ids_in = sem("ids_in")
        ident_in = sem("ident_in")
        idx_set = sem("idx_set")
        gathered = sem("gathered")
        transposed = sem("transposed")
        xt_copied = sem("xt_copied")
        xt_stored = [sem(f"xt_stored{g}") for g in range(2)]
        pair_in = sem("pair_in")
        feat_in = [sem(f"feat_in{k}") for k in range(2)]
        hid_in = [sem(f"hid_in{k}") for k in range(2)]
        z0_made = sem("z0_made")
        zp_made = sem("zp_made")
        zs_made = sem("zs_made")
        hi_made = sem("hi_made")
        lo_made = sem("lo_made")
        cur0_done = sem("cur0_done")
        zp_used = sem("zp_used")
        split_used = sem("split_used")
        hidden_out = sem("hidden_out")
        hidden_stored = [sem(f"hidden_stored{k}") for k in range(2)]
        sum0_done = sem("sum0_done")
        sum1_done = sem("sum1_done")
        pooled = sem("pooled")
        mlp_mm = sem("mlp_mm")
        mlp_act = sem("mlp_act")
        y_stored = sem("y_stored")

        block = ctx.enter_context(nc.Block())

        def batches(engine, body):
            body(0, True, False)
            with engine.Fori(1, BATCHES - 1) as b:
                body(b, False, False)
            body(BATCHES - 1, False, True)

        mlp_groups = ([(h, 1, m) for h in range(2) for m in range(TOP1 // P)]
                      + [(h, 2, m) for h in range(2) for m in range(TOP2 // P)]
                      + [(h, 3, 0) for h in range(2)])

        @block.gpsimd
        def _(pool):
            def gather(indices):
                for f in range(FIELDS):
                    nc.gpsimd.indirect_dma_start(
                        emb[:, f, :], None, tables[f],
                        bass.IndirectOffsetOnAxis(indices[:, f:f + 1], 0)).then_inc(gathered, 16)

            pool.wait_ge(ids_in, 16)
            gather(ids_sb[:, 0, :])
            with pool.Fori(1, BATCHES) as b:
                pool.wait_ge(gathered, 16 * FIELDS * b)
                pool.wait_ge(transposed, 2 * b)
                nc.gpsimd.tensor_copy(idx[:], ids_sb[:, bass.ds(b, 1), :].squeeze(1)).then_inc(idx_set, 1)
                pool.wait_ge(ids_in, 16)
                pool.wait_ge(idx_set, b)
                gather(idx)

        @block.sync
        def _(sp):
            sp.dma_start(ids_sb[:], ids.rearrange("(b p) f -> p b f", p=P)).then_inc(ids_in, 16)
            sp.dma_start(ident[:], identity).then_inc(ident_in, 16)
            sp.dma_start(w0_sb[:], w0_ij).then_inc(w0_in, 16)
            sp.dma_start(w0_back[:, :, 0:WIDE], w0_ji).then_inc(w0_in, 16)
            sp.dma_start(w1_sb[:], w1).then_inc(w1_in, 16)
            sp.dma_start(wt1_sb[0:HALF, 0, :], w_top1[0:HALF, :]).then_inc(mlp_in, 16)
            sp.dma_start(wt1_sb[:, 1, :], w_top1[HALF:HALF + P, :]).then_inc(mlp_in, 16)
            sp.dma_start(wt1_sb[HALF:DIRECT_DENSE, 0, :], w_top1[HALF + P:, :]).then_inc(mlp_in, 16)
            sp.dma_start(wt2_sb[:], w_top2.rearrange("(k p) m -> p k m", p=P)).then_inc(mlp_in, 16)
            sp.dma_start(wt3_sb[:], w_top3).then_inc(mlp_in, 16)
            sp.dma_start(bt1_sb[:], b_top1).then_inc(mlp_in, 16)
            sp.dma_start(bt2_sb[:], b_top2).then_inc(mlp_in, 16)
            sp.dma_start(top0[HALF:DIRECT_DENSE, :], dense_t).then_inc(mlp_in, 16)

            def batch(b, first, last, prologue=False):
                column = [b * COLS + k * U for k in range(2 * UNITS)]
                if not isinstance(b, int):
                    column = [sp.snap(c) for c in column]

                def store_xt(k):
                    sp.wait_ge(xt_copied, 2 * b + k - k // UNITS * 2 + 1)
                    g = k % UNITS
                    for row, count in ((0, FIELDS), (FIELDS, COPY_ROWS)):
                        sp.dma_start(bass.AP(xt_dram.tensor, column[k] + row * N, [[N, count], [2 * U, 2], [1, U]]),
                                     xt[0:2 * count, g, :]).then_inc(xt_stored[g], 16)

                def load_pair(k):
                    if not (prologue and k == 0):
                        sp.wait_ge(z0_made, UNITS * b + k)
                    sp.wait_ge(xt_stored[k % 2], 32 * (b + k // UNITS) + 32)
                    sp.dma_start(shifted[:], bass.AP(xt_dram.tensor, column[k], [
                        [N, FIELDS], [SHIFTS * N, CYC], [N, SHIFTS], [1, U]])).then_inc(pair_in, 16)
                    sp.dma_start(base[:], bass.AP(xt_dram.tensor, column[k], [
                        [N, FIELDS], [0, CYC], [1, U]])).then_inc(pair_in, 16)

                def load_feat(k, free=True):
                    if free:
                        sp.wait_ge(zs_made, SPLIT * (UNITS * b + k) - SPLIT)
                    sp.dma_start(feat_rep[k % 2][:], bass.AP(xt_dram.tensor, column[k], [
                        [0, GJ], [SI * N, GI], [N, SI], [1, U]])).then_inc(feat_in[k % 2], 16)

                def hidden_round(k):
                    sp.wait_ge(hidden_out, UNITS * b + k + 1)
                    sp.dma_start(h_dram[:, bass.ds(column[k], U)],
                                 hidden[k % 2][HALF:, :]).then_inc(hidden_stored[k % 2], 16)
                    sp.wait_ge(hidden_stored[k % 2], 32 * b + 16 * (k // 2) + 16)
                    for t in range(TJ):
                        sp.dma_start(hid_rep[k % 2][:, t, :], bass.AP(h_dram.tensor, column[k] + t * N, [
                            [TJ * N, GJ], [0, GI], [1, U]])).then_inc(hid_in[k % 2], 16)

                if prologue:
                    store_xt(0)
                    load_pair(0)
                    store_xt(1)
                    load_pair(1)
                    load_feat(0, free=False)
                    hidden_round(0)
                    return
                for q in range(UNITS):
                    if q + 1 < UNITS or not last:
                        load_feat(q + 1, free=not (first and q == 0))
                        if q != 2 and not (last and q + 2 >= UNITS):
                            load_pair(q + 2)
                        hidden_round(q + 1)
                    if q == 2 and not last:
                        store_xt(UNITS)
                        store_xt(UNITS + 1)
                        load_pair(UNITS)

            batch(0, True, False, prologue=True)
            batches(sp, batch)
            for h in range(2):
                sp.wait_ge(mlp_act, len(mlp_groups) - 1 + h)
                sp.dma_start(out[bass.ts(h, U), :].rearrange("b o -> o b"), y_sb[h]).then_inc(y_stored, 16)
            sp.wait_ge(y_stored, 32)
            for k in range(2):
                sp.wait_ge(xt_stored[k], 32 * BATCHES)
                sp.wait_ge(hidden_stored[k], 16 * BATCHES * UNITS // 2)

        @block.scalar
        def _(act):
            act.wait_ge(w1_in, 16)
            nc.scalar.activation(w1_hi[:], w1_sb[:, PLAIN:], ACT.Copy).then_inc(w1_rounded, 1)

            def copy_xt(b, first):
                for g in range(2):
                    act.wait_ge(transposed, 2 * b + g + 1)
                    if not first:
                        act.wait_ge(xt_stored[g], 32 * b)
                    nc.scalar.activation(xt[:, g, :], xt_ps[g][0:2 * FIELDS, :], ACT.Copy).then_inc(xt_copied, 1)

            def relu_hidden(b, q, first=False):
                act.wait_ge(cur0_done, UNITS * b + q + 1)
                if not first:
                    act.wait_ge(hidden_stored[q % 2], 32 * b + 16 * (q // 2))
                nc.scalar.activation(hidden[q % 2][HALF:, :], cur0[q % 2][HALF:, :], ACT.Relu).then_inc(hidden_out, 1)

            copy_xt(0, True)
            relu_hidden(0, 0, first=True)

            def batch(b, first, last):
                for q in range(UNITS):
                    if q + 1 < UNITS or not last:
                        nb, nq = (b, q + 1) if q + 1 < UNITS else (b + 1, 0)
                        relu_hidden(nb, nq, first=first and q == 0)
                    if q == 2 and not last:
                        copy_xt(b + 1, False)
                    for k in range(SPLIT):
                        act.wait_ge(zs_made, SPLIT * (UNITS * b + q) + k + 1)
                        if not (first and q == 0):
                            act.wait_ge(split_used, SPLIT * (UNITS * b + q) - SPLIT + k + 1)
                        nc.scalar.activation(z_hi[k][:], zs[k][:], ACT.Copy).then_inc(hi_made, 1)
            batches(act, batch)

            act.wait_ge(mlp_in, 16 * 8)
            for n, (h, layer, m) in enumerate(mlp_groups):
                act.wait_ge(mlp_mm, n + 1)
                src = mlp_ps[n % 2]
                if layer == 1:
                    nc.scalar.activation(act1[h][:, m, :], src[:], ACT.Relu, bias=bt1_sb[:, m:m + 1]).then_inc(mlp_act, 1)
                elif layer == 2:
                    nc.scalar.activation(act2[h][:, m, :], src[:], ACT.Relu, bias=bt2_sb[:, m:m + 1]).then_inc(mlp_act, 1)
                else:
                    nc.scalar.activation(y_sb[h], src[0:1, :], ACT.Copy).then_inc(mlp_act, 1)

        @block.vector
        def _(dve):
            dve.wait_ge(w0_in, 32)
            nc.vector.tensor_tensor(w0_sb[:], w0_sb[:], w0_back[:, :, 0:WIDE], ALU.add).then_inc(w0_folded, 1)
            dve.wait_ge(w1_rounded, 1)
            nc.vector.tensor_tensor(w1_lo[:], w1_sb[:, PLAIN:], w1_hi[:].bitcast(f32), ALU.subtract).then_inc(w1_split, 1)

            def make_z0(b, q, first=False):
                dve.wait_ge(pair_in, 32 * (UNITS * b + q) + 32)
                if first:
                    dve.wait_ge(w0_folded, 1)
                else:
                    dve.wait_ge(cur0_done, UNITS * b + q)
                nc.vector.tensor_tensor(z0[:], shifted[:], base[:].unsqueeze(1).broadcast_to([PAIR0, SHIFTS, U]), ALU.mult).then_inc(z0_made, 1)

            def product(out_, b, q, t):
                hid = hid_rep[q % 2][:, t, :].unsqueeze(1).broadcast_to([P, SI, U])
                return nc.vector.tensor_tensor(out_, feat_rep[q % 2][:], hid, ALU.mult)

            def add_up(total, cur, part, n, q, done, start):
                if start:
                    nc.vector.tensor_scalar(total[:], cur[0:part, :], 0.0, None, ALU.max).then_inc(done, 1)
                else:
                    dve.wait_ge(done, n)
                    nc.vector.scalar_tensor_tensor(total[:], cur[0:part, :], 0.0, total[:], ALU.max, ALU.add).then_inc(done, 1)

            def pool_batch(dst, total, b, done):
                dve.wait_ge(done, UNITS * b + UNITS)
                nc.vector.tensor_reduce(dst, total[:].rearrange("p (d s) -> p s d", d=DPU), AX.X, ALU.add).then_inc(pooled, 1)

            def sum_direct(b, q, first=False):
                dve.wait_ge(cur0_done, UNITS * b + q + 1)
                if q == 0 and not first:
                    dve.wait_ge(pooled, 2 * b - 1)
                add_up(sum0, cur0[q % 2], HALF, UNITS * b + q, q, sum0_done, q == 0)
                if q == UNITS - 1:
                    pool_batch(top0[0:HALF, bass.ts(b, P)], sum0, b, sum0_done)

            def sum_layer1(b, q, first=False):
                dve.wait_ge(split_used, SPLIT * (UNITS * b + q) + SPLIT)
                if q == 0 and not first:
                    dve.wait_ge(pooled, 2 * b)
                add_up(sum1, cur1[q % 2], P, UNITS * b + q, q, sum1_done, q == 0)
                if q == UNITS - 1:
                    pool_batch(top1[:, bass.ts(b, P)], sum1, b, sum1_done)

            make_z0(0, 0, first=True)
            sum_direct(0, 0, first=True)

            def batch(b, first, last):
                for q in range(UNITS):
                    ahead = q + 1 < UNITS or not last
                    nb, nq = (b, q + 1) if q + 1 < UNITS else (b + 1, 0)
                    begin = first and q == 0
                    if ahead:
                        make_z0(nb, nq)
                    dve.wait_ge(feat_in[q % 2], 32 * b + 16 * (q // 2) + 16)
                    dve.wait_ge(hid_in[q % 2], 16 * TJ * (2 * b + q // 2 + 1))
                    for t in range(PLAIN):
                        if not begin:
                            dve.wait_ge(zp_used, PLAIN * (UNITS * b + q) - PLAIN + t + 1)
                        product(zp[t][:], b, q, t).then_inc(zp_made, 1)
                    for k in range(SPLIT):
                        if not begin:
                            dve.wait_ge(lo_made, SPLIT * (UNITS * b + q) - SPLIT + k + 1)
                        product(zs[k][:], b, q, PLAIN + k).then_inc(zs_made, 1)
                    if not begin:
                        sum_layer1(*((b, q - 1) if q else (b - 1, UNITS - 1)), first=first)
                    for k in range(SPLIT):
                        dve.wait_ge(hi_made, SPLIT * (UNITS * b + q) + k + 1)
                        if not begin:
                            dve.wait_ge(split_used, SPLIT * (UNITS * b + q) - SPLIT + k + 1)
                        nc.vector.tensor_tensor(z_lo[k][:], zs[k][:], z_hi[k][:].bitcast(f32), ALU.subtract).then_inc(lo_made, 1)
                    if ahead:
                        sum_direct(nb, nq)
            batches(dve, batch)
            sum_layer1(BATCHES - 1, UNITS - 1)

        @block.tensor
        def _(pe):
            def transpose(b, first):
                pe.wait_ge(gathered, 16 * FIELDS * b + 16 * FIELDS)
                pe.wait_ge(ident_in, 16)
                rows = emb[:].rearrange("p f (e d) -> p (f e) d", e=2)
                for g in range(2):
                    if not first:
                        pe.wait_ge(xt_copied, 2 * b - 1 + g)
                    for d in range(DPU):
                        last = nc.tensor.transpose(xt_ps[g][0:2 * FIELDS, d * P:(d + 1) * P],
                                                   rows[:, :, g * DPU + d], ident[:])
                    last.then_inc(transposed, 1)

            def layer0(b, q, first=False, second=False):
                pe.wait_ge(z0_made, UNITS * b + q + 1)
                if not (first or second):
                    pe.wait_ge(hidden_out, UNITS * b + q - 1)
                    pe.wait_ge(sum0_done, UNITS * b + q - 1)
                for t in range(SHIFTS):
                    last = nc.tensor.matmul(cur0[q % 2][:], w0_sb[:, t, :], z0[:, t, :],
                                            start=t == 0, stop=t == SHIFTS - 1)
                last.then_inc(cur0_done, 1)

            def layer1(b, q, begin):
                bank = cur1[q % 2]
                for t in range(PLAIN):
                    pe.wait_ge(zp_made, PLAIN * (UNITS * b + q) + t + 1)
                    if t == 0 and not begin:
                        pe.wait_ge(sum1_done, UNITS * b + q - 1)
                    for s in range(SI):
                        last = nc.tensor.matmul(bank[:], w1_sb[:, t, s, :], zp[t][:, s, :],
                                                start=t == 0 and s == 0, stop=False)
                    last.then_inc(zp_used, 1)
                for k in range(SPLIT):
                    pe.wait_ge(hi_made, SPLIT * (UNITS * b + q) + k + 1)
                    for s in range(SI):
                        nc.tensor.matmul(bank[:], w1_hi[:, k, s, :], z_hi[k][:, s, :], start=False, stop=False)
                        nc.tensor.matmul(bank[:], w1_lo[:, k, s, :], z_hi[k][:, s, :], start=False, stop=False)
                    pe.wait_ge(lo_made, SPLIT * (UNITS * b + q) + k + 1)
                    for s in range(SI):
                        end = k == SPLIT - 1 and s == SI - 1
                        last = nc.tensor.matmul(bank[:], w1_hi[:, k, s, :], z_lo[k][:, s, :], start=False, stop=end)
                    last.then_inc(split_used, 1)

            transpose(0, True)
            pe.wait_ge(w0_folded, 1)
            layer0(0, 0, first=True)
            pe.wait_ge(w1_split, 1)

            def batch(b, first, last):
                for q in range(UNITS):
                    if q + 1 < UNITS or not last:
                        nb, nq = (b, q + 1) if q + 1 < UNITS else (b + 1, 0)
                        layer0(nb, nq, second=first and q == 0)
                    if q == 2 and not last:
                        transpose(b + 1, False)
                    layer1(b, q, first and q < 2)
            batches(pe, batch)

            pe.wait_ge(pooled, 2 * BATCHES)
            done = {g: n for n, g in enumerate(mlp_groups)}
            for n, (h, layer, m) in enumerate(mlp_groups):
                if n >= 2:
                    pe.wait_ge(mlp_act, n - 1)
                cols = slice(h * U, (h + 1) * U)
                if layer == 1:
                    nc.tensor.matmul(mlp_ps[n % 2][:], wt1_sb[0:DIRECT_DENSE, 0, m * P:(m + 1) * P], top0[:, cols], start=True, stop=False)
                    last = nc.tensor.matmul(mlp_ps[n % 2][:], wt1_sb[:, 1, m * P:(m + 1) * P], top1[:, cols], start=False, stop=True)
                elif layer == 2:
                    pe.wait_ge(mlp_act, done[(h, 1, TOP1 // P - 1)] + 1)
                    for k in range(TOP1 // P):
                        last = nc.tensor.matmul(mlp_ps[n % 2][:], wt2_sb[:, k, m * P:(m + 1) * P], act1[h][:, k, :], start=k == 0, stop=k == TOP1 // P - 1)
                else:
                    pe.wait_ge(mlp_act, done[(h, 2, TOP2 // P - 1)] + 1)
                    for k in range(TOP2 // P):
                        last = nc.tensor.matmul(mlp_ps[n % 2][0:1, :], wt3_sb[:, k:k + 1], act2[h][:, k, :], start=k == 0, stop=k == TOP2 // P - 1)
                last.then_inc(mlp_mm, 1)


def pair_rows():
    ij = np.full((FIELDS, CYC, SHIFTS), -1)
    ji = ij.copy()
    for i in range(FIELDS):
        for c in range(CYC):
            for t in range(SHIFTS):
                far = SHIFTS * c + t
                j = (i + far) % FIELDS
                if far <= FIELDS // 2:
                    ij[i, c, t] = i * FIELDS + j
                    if far:
                        ji[i, c, t] = j * FIELDS + i
    return ij.reshape(PAIR0, SHIFTS), ji.reshape(PAIR0, SHIFTS)


def kernel(**inputs):
    import concourse.bacc as bacc
    from concourse.bass_utils import run_bass_kernel_spmd

    a = {k: np.asarray(v) for k, v in inputs.items()}
    w0 = a["L0_rec_W0"]
    w0 = np.concatenate([np.concatenate([w0[:, HALF:], w0[:, :HALF]], 1), np.zeros((1, WIDE), w0.dtype)])
    ij, ji = pair_rows()
    w1 = a["L0_rec_W1"].reshape(FIELDS, HALF, WIDE)
    w1 = np.concatenate([w1, np.zeros((GI * SI - FIELDS, HALF, WIDE), w1.dtype)])
    w1 = w1.reshape(GI, SI, GJ, TJ, WIDE).transpose(2, 0, 3, 1, 4).reshape(P, TJ, SI, WIDE)
    arrays = {f"tbl_{f}": a[f"tbl_{f}"] for f in range(FIELDS)}
    arrays |= {
        "ids": a["ids"], "w0_ij": w0[ij], "w0_ji": w0[ji], "w1": w1, "dense_t": a["dense_ctx"].T,
        "w_top1": a["W_top1"], "w_top2": a["W_top2"],
        "b_top1": a["b_top1"].reshape(-1, P).T, "b_top2": a["b_top2"].reshape(-1, P).T,
        "w_top3": a["W_top3"].reshape(-1, P).T, "identity": np.eye(P, dtype=np.float32),
    }
    arrays = {k: np.ascontiguousarray(v) for k, v in arrays.items()}

    nc = bacc.Bacc("TRN2", target_bir_lowering=False, num_devices=1)
    aps = {k: nc.dram_tensor(k, v.shape, mybir.dt.from_np(v.dtype), kind="ExternalInput").ap() for k, v in arrays.items()}
    out = nc.dram_tensor("out", (BATCH, 1), mybir.dt.float32, kind="ExternalOutput").ap()
    tables = [aps.pop(f"tbl_{f}") for f in range(FIELDS)]
    tower(nc, tables, out=out, **aps)
    r = run_bass_kernel_spmd(nc, [arrays], core_ids=[0])
    return r.results[0]["out"]
```

```python
from contextlib import ExitStack

import numpy as np
import concourse.bass as bass
from concourse import mybir

FIELDS, DIM, BATCH = 39, 16, 1024
HALF, WIDE = 64, 128
DENSE, TOP1, TOP2 = 16, 512, 256
P = 128
U = 512
S = U // DIM
UNITS = BATCH // S
RU = 4
ROUNDS = UNITS // RU
CYC, SHIFTS = 3, 7
PAIR0 = FIELDS * CYC
PARTS0 = [(0, 3), (3, SHIFTS)]
ROWS = FIELDS + CYC * SHIFTS - 1
GI, SI = 8, 5
GJ, TJ = 16, 4
FB, FG = P // S, 10
PLAIN = 2
SPLIT = TJ - PLAIN
SPLIT_TILES = [SI - 1, SI]
DIRECT_DENSE = HALF + DENSE
CHUNKS = [(0, 352), (352, 352), (704, 320)]


def tower(nc, table, ids, id_base, w0_ij, w0_ji, w1, dense_t, w_top1, b_top1, w_top2, b_top2,
          w_top3, out):
    f32, f32r, i32 = mybir.dt.float32, mybir.dt.float32r, mybir.dt.int32
    ALU, ACT, AX = mybir.AluOpType, mybir.ActivationFunctionType, mybir.AxisListType

    x_dram = nc.dram_tensor("x_dram", (UNITS, ROWS, U), f32, kind="Internal").ap()
    h_dram = nc.dram_tensor("h_dram", (UNITS, HALF, U), f32, kind="Internal").ap()
    X_UNIT, H_UNIT = ROWS * U, HALF * U

    with ExitStack() as ctx:
        def sb(name, shape, dtype=f32):
            return ctx.enter_context(nc.sbuf_tensor(name, shape, dtype))

        def ps(name, shape):
            return ctx.enter_context(nc.psum_tensor(name, shape, f32))

        def sem(name):
            return ctx.enter_context(nc.semaphore(name))

        w0_sb = sb("w0_sb", [PAIR0, SHIFTS, WIDE])
        w1_sb = sb("w1_sb", [P, PLAIN, SI, WIDE])
        w1_rest = sb("w1_rest", [P, WIDE])
        w1_hi = sb("w1_hi", [P, SPLIT, SI, WIDE], f32r)
        w1_lo = sb("w1_lo", [P, SPLIT, SI, WIDE], f32r)
        wt1_sb = sb("wt1_sb", [P, 2, TOP1])
        wt2_sb = sb("wt2_sb", [P, TOP1 // P, TOP2])
        wt3_sb = sb("wt3_sb", [P, TOP2 // P])
        bt1_sb = sb("bt1_sb", [P, TOP1 // P])
        bt2_sb = sb("bt2_sb", [P, TOP2 // P])
        ids_sb = sb("ids_sb", [P, UNITS * FG], i32)
        base_sb = sb("base_sb", [P, FG], i32)
        rows_sb = ids_sb
        idx = sb("idx", [P, RU * FG], i32)
        emb = [sb(f"emb{q}", [P, FG, DIM]) for q in range(RU)]
        base = sb("base", [PAIR0, U])
        shifted = sb("shifted", [PAIR0, SHIFTS, U])
        feat_rep = [sb(f"feat_rep{k}", [P, SI, U]) for k in range(2)]
        hid_rep = [sb(f"hid_rep{k}", [P, TJ, U]) for k in range(2)]
        z0 = sb("z0", [PAIR0, SHIFTS, U])
        zp = [sb(f"zp{k}", [P, SI, U]) for k in range(PLAIN)]
        zs = [sb(f"zs{k}", [P, SI, U]) for k in range(SPLIT)]
        z_hi = [sb(f"z_hi{k}", [P, SI, U], f32r) for k in range(SPLIT)]
        z_lo = [sb(f"z_lo{k}", [P, SI, U], f32r) for k in range(SPLIT)]
        act0 = [sb(f"act0_{k}", [P, U]) for k in range(2)]
        act1 = sb("act1", [P, U])
        low = sb("low", [P, BATCH])
        top0 = low[0:DIRECT_DENSE, :]
        y_sb = low[96:97, :]
        top1 = sb("top1", [P, BATCH])
        h1 = [sb(f"h1_{k}", [P, TOP1 // P, CHUNKS[0][1]]) for k in range(2)]
        h2 = [sb(f"h2_{k}", [P, TOP2 // P, CHUNKS[0][1]]) for k in range(2)]
        w0_back = z0[:, :, 0:WIDE]
        w1_whole = zs[0][:].rearrange("p s u -> p (s u)")[:, 0:SPLIT * SI * WIDE].rearrange("p (t s l) -> p t s l", t=SPLIT, s=SI)

        cur0 = [ps(f"cur0_{k}", [P, U]) for k in range(2)]
        cur1 = [ps(f"cur1_{k}", [P, U]) for k in range(2)]
        mlp_ps = [ps(f"mlp_ps{k}", [P, U]) for k in range(4)]

        ids_in = sem("ids_in")
        rows_made = sem("rows_made")
        idx_set = sem("idx_set")
        w0_in = sem("w0_in")
        w1_in = sem("w1_in")
        mlp_in = sem("mlp_in")
        w0_folded = sem("w0_folded")
        w1_rounded = sem("w1_rounded")
        w1_split = sem("w1_split")
        gathered = [sem(f"gathered{q}") for q in range(RU)]
        x_stored = [sem(f"x_stored{q}") for q in range(RU)]
        base_in = sem("base_in")
        shifted_in = [sem(f"shifted_in{n}") for n in range(len(PARTS0))]
        feat_in = [sem(f"feat_in{k}") for k in range(2)]
        hid_in = [sem(f"hid_in{k}") for k in range(2)]
        z0_made = sem("z0_made")
        zp_made = sem("zp_made")
        zs_made = sem("zs_made")
        hi_made = sem("hi_made")
        lo_made = sem("lo_made")
        cur0_done = sem("cur0_done")
        zp_used = sem("zp_used")
        split_used = sem("split_used")
        act0_done = sem("act0_done")
        act1_done = sem("act1_done")
        h_stored = [sem(f"h_stored{k}") for k in range(2)]
        sum0_done = sem("sum0_done")
        sum1_done = sem("sum1_done")
        mlp_mm = sem("mlp_mm")
        mlp_act = sem("mlp_act")
        y_stored = sem("y_stored")
        X_STORES = FB + 2

        block = ctx.enter_context(nc.Block())

        def rounds(engine, body):
            body(0, True, False)
            with engine.Fori(1, ROUNDS - 1) as r:
                body(r, False, False)
            body(ROUNDS - 1, False, True)

        def groups(chunks, layer):
            return [(c, layer, m) for c in chunks for m in range({1: TOP1 // P, 2: TOP2 // P, 3: 1}[layer])]
        turns = [groups([0, 1], 1), groups([0, 1], 2), groups([0], 3),
                 groups([2], 1) + groups([1], 3) + groups([2], 2) + groups([2], 3)]
        order = [g for turn in turns for g in turn]
        place = {g: n for n, g in enumerate(order)}

        @block.gpsimd
        def _(pool):
            def gather(q, indices):
                for g in range(FG):
                    nc.gpsimd.indirect_dma_start(
                        emb[q][:, g, :], None, table,
                        bass.IndirectOffsetOnAxis(indices[:, g:g + 1], 0)).then_inc(gathered[q], 16)

            pool.wait_ge(rows_made, 1)
            for q in range(RU):
                gather(q, rows_sb[:, q * FG:(q + 1) * FG])
            with pool.Fori(1, ROUNDS) as r:
                for q in range(RU):
                    pool.wait_ge(gathered[q], 16 * FG * r)
                    pool.wait_ge(x_stored[q], 16 * X_STORES * r)
                nc.gpsimd.tensor_copy(idx[:], rows_sb[:, bass.ts(r, RU * FG)]).then_inc(idx_set, 1)
                pool.wait_ge(rows_made, 1)
                pool.wait_ge(idx_set, r)
                for q in range(RU):
                    gather(q, idx[:, q * FG:(q + 1) * FG])

        @block.sync
        def _(sp):
            sp.dma_start(ids_sb[:], ids).then_inc(ids_in, 16)
            sp.dma_start(base_sb[:], id_base).then_inc(ids_in, 16)
            sp.dma_start(w0_sb[:], w0_ij).then_inc(w0_in, 16)
            sp.dma_start(w0_back, w0_ji).then_inc(w0_in, 16)
            sp.dma_start(w1_whole, w1[:, PLAIN:]).then_inc(w1_in, 16)
            sp.dma_start(w1_sb[:], w1[:, 0:PLAIN]).then_inc(w1_in, 16)
            sp.dma_start(w1_rest[:], w1[:, PLAIN, SPLIT_TILES[0]]).then_inc(w1_in, 16)

            def body(r, first, last, prologue=False):
                x_at = [(RU * r + k) * X_UNIT for k in range(RU + 3)]
                h_at = [(RU * r + k) * H_UNIT for k in range(RU + 1)]
                if not isinstance(r, int):
                    x_at = [sp.snap(x) for x in x_at]
                    h_at = [sp.snap(x) for x in h_at]

                def store_x(k):
                    q = k % RU
                    sp.wait_ge(gathered[q], 16 * FG * (r + k // RU) + 16 * FG)
                    for row, fb, g in [(FG * fb, fb, 0) for fb in range(FB)] + [(FIELDS + 1, 0, 1), (FIELDS + FG, 1, 0)]:
                        sp.dma_start(bass.AP(x_dram.tensor, x_at[k] + row * U, [[DIM, S], [U, FG - g], [1, DIM]]),
                                     emb[q][fb * S:(fb + 1) * S, g:, :]).then_inc(x_stored[q], 16)

                def load_pair(k, between=lambda: None):
                    if not (prologue and k == 0):
                        sp.wait_ge(z0_made, len(PARTS0) * (RU * r + k))
                    sp.wait_ge(x_stored[k % RU], 16 * X_STORES * (r + k // RU) + 16 * X_STORES)
                    sp.dma_start(base[:], bass.AP(x_dram.tensor, x_at[k], [
                        [U, FIELDS], [0, CYC], [1, U]])).then_inc(base_in, 16)
                    for n, (t0, t1) in enumerate(PARTS0):
                        if n == len(PARTS0) - 1:
                            between()
                        sp.dma_start(shifted[:, t0:t1, :], bass.AP(x_dram.tensor, x_at[k] + t0 * U, [
                            [U, FIELDS], [SHIFTS * U, CYC], [1, (t1 - t0) * U]])).then_inc(shifted_in[n], 16)

                def load_feat(k, free=True):
                    if free:
                        sp.wait_ge(zs_made, SPLIT * (RU * r + k) - SPLIT)
                    sp.dma_start(feat_rep[k % 2][:], bass.AP(x_dram.tensor, x_at[k], [
                        [0, GJ], [SI * U, GI], [1, SI * U]])).then_inc(feat_in[k % 2], 16)

                def store_hidden(k):
                    sp.wait_ge(act0_done, RU * r + k + 1)
                    sp.dma_start(bass.AP(h_dram.tensor, h_at[k], [[U, HALF], [1, U]]),
                                 act0[k % 2][HALF:, :]).then_inc(h_stored[k % 2], 16)

                def load_hidden(k):
                    sp.wait_ge(h_stored[k % 2], 16 * (RU // 2) * r + 16 * (k // 2) + 16)
                    sp.dma_start(hid_rep[k % 2][:], bass.AP(h_dram.tensor, h_at[k], [
                        [TJ * U, GJ], [0, GI], [1, TJ * U]])).then_inc(hid_in[k % 2], 16)

                if prologue:
                    store_x(0)
                    load_pair(0)
                    store_x(1)
                    load_feat(0, free=False)
                    load_pair(1, between=lambda: store_hidden(0))
                    load_hidden(0)
                    store_x(2)
                    return
                for q in range(RU):
                    if q + 1 < RU or not last:
                        load_feat(q + 1, free=not (first and q == 0))
                    if q + 2 < RU or not last:
                        load_pair(q + 2)
                    if q + 1 < RU or not last:
                        store_hidden(q + 1)
                        load_hidden(q + 1)
                    if q + 3 < RU or not last:
                        store_x(q + 3)

            body(0, True, False, prologue=True)
            sp.dma_start(wt1_sb[0:HALF, 0, :], w_top1[0:HALF, :]).then_inc(mlp_in, 16)
            sp.dma_start(wt1_sb[:, 1, :], w_top1[HALF:HALF + P, :]).then_inc(mlp_in, 16)
            sp.dma_start(wt1_sb[HALF:DIRECT_DENSE, 0, :], w_top1[HALF + P:, :]).then_inc(mlp_in, 16)
            sp.dma_start(wt2_sb[:], w_top2.rearrange("(k p) m -> p k m", p=P)).then_inc(mlp_in, 16)
            sp.dma_start(wt3_sb[:], w_top3).then_inc(mlp_in, 16)
            sp.dma_start(bt1_sb[:], b_top1).then_inc(mlp_in, 16)
            sp.dma_start(bt2_sb[:], b_top2).then_inc(mlp_in, 16)
            sp.dma_start(top0[HALF:DIRECT_DENSE, :], dense_t).then_inc(mlp_in, 16)
            rounds(sp, body)
            sp.wait_ge(mlp_act, len(order))
            sp.dma_start(out.rearrange("b o -> o b"), y_sb[:]).then_inc(y_stored, 16)
            sp.wait_ge(y_stored, 16)
            for q in range(RU):
                sp.wait_ge(x_stored[q], 16 * X_STORES * ROUNDS)
            for k in range(2):
                sp.wait_ge(h_stored[k], 16 * UNITS // 2)

        @block.scalar
        def _(act):
            act.wait_ge(w1_in, 48)
            nc.scalar.activation(w1_hi[:], w1_whole, ACT.Copy).then_inc(w1_rounded, 1)

            def relu0(r, k, begin=False):
                act.wait_ge(cur0_done, RU * r + k + 1)
                if not begin:
                    act.wait_ge(h_stored[k % 2], 16 * (RU // 2) * r + 16 * (k // 2))
                    act.wait_ge(sum0_done, RU * r + k - 1)
                nc.scalar.activation(act0[k % 2][:], cur0[k % 2][:], ACT.Relu).then_inc(act0_done, 1)

            def relu1(r, k, begin=False):
                act.wait_ge(split_used, SPLIT * (RU * r + k) + SPLIT)
                if not begin:
                    act.wait_ge(sum1_done, RU * r + k)
                nc.scalar.activation(act1[:], cur1[k % 2][:], ACT.Relu).then_inc(act1_done, 1)

            def mlp(turn):
                for g in turn:
                    c, layer, m = g
                    n, width = place[g], CHUNKS[c][1]
                    act.wait_ge(mlp_mm, n + 1)
                    src = mlp_ps[n % 4]
                    if layer == 1:
                        nc.scalar.activation(h1[c % 2][:, m, 0:width], src[:, 0:width], ACT.Relu, bias=bt1_sb[:, m:m + 1]).then_inc(mlp_act, 1)
                    elif layer == 2:
                        nc.scalar.activation(h2[c % 2][:, m, 0:width], src[:, 0:width], ACT.Relu, bias=bt2_sb[:, m:m + 1]).then_inc(mlp_act, 1)
                    else:
                        at = CHUNKS[c][0]
                        nc.scalar.activation(y_sb[:, at:at + width], src[0:1, 0:width], ACT.Copy).then_inc(mlp_act, 1)

            def body(r, first, last):
                for q in range(RU):
                    begin = first and q == 0
                    if not begin:
                        relu1(r, q - 1, begin=first and q == 1)
                    if q + 1 < RU or not last:
                        relu0(r, q + 1, begin=begin)
                    for k in range(SPLIT):
                        act.wait_ge(zs_made, SPLIT * (RU * r + q) + k + 1)
                        if not begin:
                            act.wait_ge(split_used, SPLIT * (RU * r + q) - SPLIT + k + 1)
                        n = SPLIT_TILES[k]
                        nc.scalar.activation(z_hi[k][:, 0:n], zs[k][:, 0:n], ACT.Copy).then_inc(hi_made, 1)
                    if last and q < 2:
                        if q == 0:
                            act.wait_ge(mlp_in, 16 * 8)
                        mlp(turns[q])

            relu0(0, 0, begin=True)
            rounds(act, body)
            relu1(ROUNDS - 1, RU - 1)
            mlp(turns[2])
            mlp(turns[3])

        @block.vector
        def _(dve):
            dve.wait_ge(ids_in, 32)
            nc.vector.tensor_tensor(rows_sb[:].rearrange("p (u g) -> p u g", g=FG), ids_sb[:].rearrange("p (u g) -> p u g", g=FG),
                                    base_sb[:].unsqueeze(1).broadcast_to([P, UNITS, FG]), ALU.add).then_inc(rows_made, 1)
            dve.wait_ge(w0_in, 32)
            nc.vector.tensor_tensor(w0_sb[:], w0_sb[:], w0_back, ALU.add).then_inc(w0_folded, 1)
            dve.wait_ge(w1_rounded, 1)
            nc.vector.tensor_tensor(w1_lo[:], w1_whole, w1_hi[:].bitcast(f32), ALU.subtract).then_inc(w1_split, 1)

            def make_z0(r, k, begin=False):
                dve.wait_ge(base_in, 16 * (RU * r + k) + 16)
                if begin:
                    dve.wait_ge(w0_folded, 1)
                else:
                    dve.wait_ge(cur0_done, RU * r + k)
                for n, (t0, t1) in enumerate(PARTS0):
                    dve.wait_ge(shifted_in[n], 16 * (RU * r + k) + 16)
                    nc.vector.tensor_tensor(z0[:, t0:t1, :], shifted[:, t0:t1, :],
                                            base[:].unsqueeze(1).broadcast_to([PAIR0, t1 - t0, U]), ALU.mult).then_inc(z0_made, 1)

            def product(out_, q, t):
                hid = hid_rep[q % 2][:, t, :].unsqueeze(1).broadcast_to([P, SI, U])
                return nc.vector.tensor_tensor(out_, feat_rep[q % 2][:], hid, ALU.mult)

            def samples(r, k):
                return bass.ds((RU * r + k) * S, S)

            def sum0(r, k):
                dve.wait_ge(act0_done, RU * r + k + 1)
                nc.vector.tensor_reduce(top0[0:HALF, samples(r, k)], act0[k % 2][0:HALF, :].rearrange("p (s d) -> p s d", d=DIM), AX.X, ALU.add).then_inc(sum0_done, 1)

            def sum1(r, k):
                dve.wait_ge(act1_done, RU * r + k + 1)
                nc.vector.tensor_reduce(top1[:, samples(r, k)], act1[:].rearrange("p (s d) -> p s d", d=DIM), AX.X, ALU.add).then_inc(sum1_done, 1)

            make_z0(0, 0, begin=True)
            sum0(0, 0)

            def body(r, first, last):
                for q in range(RU):
                    begin = first and q == 0
                    unit = RU * r + q
                    if q + 1 < RU or not last:
                        make_z0(r, q + 1)
                    dve.wait_ge(feat_in[q % 2], 16 * (RU // 2) * r + 16 * (q // 2) + 16)
                    dve.wait_ge(hid_in[q % 2], 16 * (RU // 2) * r + 16 * (q // 2) + 16)
                    for t in range(PLAIN):
                        if not begin:
                            dve.wait_ge(zp_used, (PLAIN + 1) * (unit - 1) + t + 1)
                        product(zp[t][:], q, t).then_inc(zp_made, 1)
                    for k in range(SPLIT):
                        if not begin:
                            dve.wait_ge(lo_made, SPLIT * unit - SPLIT + k + 1)
                            if k == 0:
                                dve.wait_ge(zp_used, (PLAIN + 1) * unit)
                        elif k == 0:
                            dve.wait_ge(w1_split, 1)
                        product(zs[k][:], q, PLAIN + k).then_inc(zs_made, 1)
                    if not begin:
                        sum1(r, q - 1)
                    for k in range(SPLIT):
                        dve.wait_ge(hi_made, SPLIT * unit + k + 1)
                        if not begin:
                            dve.wait_ge(split_used, SPLIT * unit - SPLIT + k + 1)
                        n = SPLIT_TILES[k]
                        nc.vector.tensor_tensor(z_lo[k][:, 0:n], zs[k][:, 0:n], z_hi[k][:, 0:n].bitcast(f32), ALU.subtract).then_inc(lo_made, 1)
                    if q + 1 < RU or not last:
                        sum0(r, q + 1)
            rounds(dve, body)
            sum1(ROUNDS - 1, RU - 1)

        @block.tensor
        def _(pe):
            def layer0(r, k, begin=False):
                if not begin:
                    pe.wait_ge(act0_done, RU * r + k - 1)
                for n, (t0, t1) in enumerate(PARTS0):
                    pe.wait_ge(z0_made, len(PARTS0) * (RU * r + k) + n + 1)
                    for t in range(t0, t1):
                        last = nc.tensor.matmul(cur0[k % 2][:], w0_sb[:, t, :], z0[:, t, :],
                                                start=t == 0, stop=t == SHIFTS - 1)
                last.then_inc(cur0_done, 1)

            def layer1(r, q, begin):
                bank = cur1[q % 2]
                unit = RU * r + q
                for t in range(PLAIN):
                    pe.wait_ge(zp_made, PLAIN * unit + t + 1)
                    if t == 0 and not begin:
                        pe.wait_ge(act1_done, unit - 1)
                    for s in range(SI):
                        last = nc.tensor.matmul(bank[:], w1_sb[:, t, s, :], zp[t][:, s, :],
                                                start=t == 0 and s == 0, stop=False)
                    last.then_inc(zp_used, 1)
                pe.wait_ge(zs_made, SPLIT * unit + 1)
                nc.tensor.matmul(bank[:], w1_rest[:], zs[0][:, SPLIT_TILES[0], :], start=False, stop=False).then_inc(zp_used, 1)
                for k in range(SPLIT):
                    pe.wait_ge(hi_made, SPLIT * unit + k + 1)
                    for s in range(SPLIT_TILES[k]):
                        nc.tensor.matmul(bank[:], w1_hi[:, k, s, :], z_hi[k][:, s, :], start=False, stop=False)
                        nc.tensor.matmul(bank[:], w1_lo[:, k, s, :], z_hi[k][:, s, :], start=False, stop=False)
                    pe.wait_ge(lo_made, SPLIT * unit + k + 1)
                    for s in range(SPLIT_TILES[k]):
                        end = k == SPLIT - 1 and s == SPLIT_TILES[k] - 1
                        last = nc.tensor.matmul(bank[:], w1_hi[:, k, s, :], z_lo[k][:, s, :], start=False, stop=end)
                    last.then_inc(split_used, 1)

            def mlp(turn):
                for g in turn:
                    c, layer, m = g
                    n, (at, width) = place[g], CHUNKS[c]
                    if n >= 4:
                        pe.wait_ge(mlp_act, n - 3)
                    bank = mlp_ps[n % 4]
                    if layer == 1:
                        for part, src in enumerate((top0, top1)):
                            last = nc.tensor.matmul(bank[:, 0:width], wt1_sb[0:src.shape[0], part, m * P:(m + 1) * P],
                                                    src[:, at:at + width], start=part == 0, stop=part == 1)
                    elif layer == 2:
                        pe.wait_ge(mlp_act, place[(c, 1, TOP1 // P - 1)] + 1)
                        for k in range(TOP1 // P):
                            last = nc.tensor.matmul(bank[:, 0:width], wt2_sb[:, k, m * P:(m + 1) * P],
                                                    h1[c % 2][:, k, 0:width], start=k == 0, stop=k == TOP1 // P - 1)
                    else:
                        pe.wait_ge(mlp_act, place[(c, 2, TOP2 // P - 1)] + 1)
                        for k in range(TOP2 // P):
                            last = nc.tensor.matmul(bank[0:1, 0:width], wt3_sb[:, k:k + 1],
                                                    h2[c % 2][:, k, 0:width], start=k == 0, stop=k == TOP2 // P - 1)
                    last.then_inc(mlp_mm, 1)

            def body(r, first, last):
                for q in range(RU):
                    if q + 1 < RU or not last:
                        layer0(r, q + 1, begin=first and q == 0)
                    if last and q < 2:
                        if q == 0:
                            pe.wait_ge(mlp_in, 16 * 8)
                            pe.wait_ge(sum0_done, CHUNKS[2][0] // S)
                            pe.wait_ge(sum1_done, CHUNKS[2][0] // S)
                        mlp(turns[q])
                    layer1(r, q, first and q < 2)

            pe.wait_ge(w0_folded, 1)
            pe.wait_ge(x_stored[0], 16 * X_STORES)
            for _ in range(8):
                nc.tensor.matmul(mlp_ps[3][:], w0_sb[:, 0, :], w0_sb[:, 0:U // WIDE, :], start=True, stop=True)
            layer0(0, 0, begin=True)
            pe.wait_ge(w1_split, 1)
            rounds(pe, body)
            mlp(turns[2])
            pe.wait_ge(sum0_done, UNITS)
            pe.wait_ge(sum1_done, UNITS)
            mlp(turns[3])


def pair_rows():
    ij = np.full((FIELDS, CYC, SHIFTS), -1)
    ji = ij.copy()
    for i in range(FIELDS):
        for c in range(CYC):
            for t in range(SHIFTS):
                far = SHIFTS * c + t
                j = (i + far) % FIELDS
                if far <= FIELDS // 2:
                    ij[i, c, t] = i * FIELDS + j
                    if far:
                        ji[i, c, t] = j * FIELDS + i
    return ij.reshape(PAIR0, SHIFTS), ji.reshape(PAIR0, SHIFTS)


def kernel(**inputs):
    import concourse.bacc as bacc
    from concourse.bass_utils import run_bass_kernel_spmd

    a = {k: np.asarray(v) for k, v in inputs.items()}
    tables = [a[f"tbl_{f}"] for f in range(FIELDS)]
    begin = np.cumsum([0] + [t.shape[0] for t in tables])[:FIELDS].astype(np.int32)
    fields = np.append(np.arange(FIELDS), 0)
    ids = a["ids"][:, fields].reshape(UNITS, S, FB, FG).transpose(2, 1, 0, 3).reshape(P, UNITS * FG)
    id_base = np.repeat(begin[fields].reshape(FB, FG), S, axis=0)
    w0 = a["L0_rec_W0"]
    w0 = np.concatenate([np.concatenate([w0[:, HALF:], w0[:, :HALF]], 1), np.zeros((1, WIDE), w0.dtype)])
    ij, ji = pair_rows()
    w1 = a["L0_rec_W1"].reshape(FIELDS, HALF, WIDE)
    w1 = np.concatenate([w1, np.zeros((GI * SI - FIELDS, HALF, WIDE), w1.dtype)])
    w1 = w1.reshape(GI, SI, GJ, TJ, WIDE).transpose(2, 0, 3, 1, 4).reshape(P, TJ, SI, WIDE)
    arrays = {
        "table": np.concatenate(tables), "ids": ids, "id_base": id_base,
        "w0_ij": w0[ij], "w0_ji": w0[ji], "w1": w1, "dense_t": a["dense_ctx"].T,
        "w_top1": a["W_top1"], "w_top2": a["W_top2"],
        "b_top1": a["b_top1"].reshape(-1, P).T, "b_top2": a["b_top2"].reshape(-1, P).T,
        "w_top3": a["W_top3"].reshape(-1, P).T,
    }
    arrays = {k: np.ascontiguousarray(v) for k, v in arrays.items()}

    nc = bacc.Bacc("TRN2", target_bir_lowering=False, num_devices=1)
    aps = {k: nc.dram_tensor(k, v.shape, mybir.dt.from_np(v.dtype), kind="ExternalInput").ap() for k, v in arrays.items()}
    out = nc.dram_tensor("out", (BATCH, 1), mybir.dt.float32, kind="ExternalOutput").ap()
    tower(nc, out=out, **aps)
    r = run_bass_kernel_spmd(nc, [arrays], core_ids=[0])
    return r.results[0]["out"]
```

```python
from contextlib import ExitStack

import numpy as np
import concourse.bass as bass
from concourse import mybir

FIELDS, DIM, BATCH = 39, 16, 1024
HALF, WIDE = 64, 128
DENSE, TOP1, TOP2 = 16, 512, 256
P = 128
U = 512
S = U // DIM
UNITS = BATCH // S
RU = 4
ROUNDS = UNITS // RU
CYC, SHIFTS = 3, 7
PAIR0 = FIELDS * CYC
PARTS0 = [(0, 3), (3, SHIFTS)]
ROWS = FIELDS + CYC * SHIFTS - 1
GI, SI = 8, 5
GJ, TJ = 16, 4
FB, FG = P // S, 10
PLAIN = 2
SPLIT = TJ - PLAIN
DIRECT_DENSE = HALF + DENSE
RS = RU * S
M1, M2 = TOP1 // P, TOP2 // P
GROUPS = M1 + M2 + 1


def tower(nc, table, ids, id_base, w0_ij, w0_ji, w1, dense_t, w_top1, b_top1, w_top2, b_top2,
          w_top3, out):
    f32, f32r, i32 = mybir.dt.float32, mybir.dt.float32r, mybir.dt.int32
    ALU, ACT, AX = mybir.AluOpType, mybir.ActivationFunctionType, mybir.AxisListType

    x_dram = nc.dram_tensor("x_dram", (UNITS, ROWS, U), f32, kind="Internal").ap()
    h_dram = nc.dram_tensor("h_dram", (UNITS, HALF, U), f32, kind="Internal").ap()
    X_UNIT, H_UNIT = ROWS * U, HALF * U

    with ExitStack() as ctx:
        def sb(name, shape, dtype=f32):
            return ctx.enter_context(nc.sbuf_tensor(name, shape, dtype))

        def ps(name, shape):
            return ctx.enter_context(nc.psum_tensor(name, shape, f32))

        def sem(name):
            return ctx.enter_context(nc.semaphore(name))

        w0_sb = sb("w0_sb", [PAIR0, SHIFTS, WIDE])
        w1_sb = sb("w1_sb", [P, PLAIN, SI, WIDE])
        w1_hi = sb("w1_hi", [P, SPLIT, SI, WIDE], f32r)
        w1_lo = sb("w1_lo", [P, SPLIT, SI, WIDE], f32r)
        wt1_sb = sb("wt1_sb", [P, 2, TOP1])
        wt2_sb = sb("wt2_sb", [P, TOP1 // P, TOP2])
        wt3_sb = sb("wt3_sb", [P, TOP2 // P])
        bt1_sb = sb("bt1_sb", [P, TOP1 // P])
        bt2_sb = sb("bt2_sb", [P, TOP2 // P])
        ids_sb = sb("ids_sb", [P, UNITS * FG], i32)
        base_sb = sb("base_sb", [P, FG], i32)
        rows_sb = ids_sb
        idx = sb("idx", [P, RU * FG], i32)
        emb = [sb(f"emb{q}", [P, FG, DIM]) for q in range(RU)]
        base = sb("base", [PAIR0, U])
        shifted = sb("shifted", [PAIR0, SHIFTS, U])
        feat_rep = [sb(f"feat_rep{k}", [P, SI, U]) for k in range(2)]
        hid_rep = [sb(f"hid_rep{k}", [P, TJ, U]) for k in range(2)]
        z0 = sb("z0", [PAIR0, SHIFTS, U])
        zp = [sb(f"zp{k}", [P, SI, U]) for k in range(PLAIN)]
        zs = [sb(f"zs{k}", [P, SI, U]) for k in range(SPLIT)]
        z_hi = [sb(f"z_hi{k}", [P, SI, U], f32r) for k in range(SPLIT)]
        z_lo = [sb(f"z_lo{k}", [P, SI, U], f32r) for k in range(SPLIT)]
        act0 = [sb(f"act0_{k}", [P, U]) for k in range(2)]
        act1 = sb("act1", [P, U])
        low = sb("low", [P, BATCH])
        top0 = low[0:DIRECT_DENSE, :]
        y_sb = low[96:97, :]
        top1 = sb("top1", [P, BATCH])
        h1 = sb("h1", [P, M1, RS])
        h2 = sb("h2", [P, M2, RS])
        w0_back = z0[:, :, 0:WIDE]
        w1_whole = zs[0][:].rearrange("p s u -> p (s u)")[:, 0:SPLIT * SI * WIDE].rearrange("p (t s l) -> p t s l", t=SPLIT, s=SI)

        cur0 = [ps(f"cur0_{k}", [P, U]) for k in range(2)]
        cur1 = [ps(f"cur1_{k}", [P, U]) for k in range(2)]
        mlp_ps = [ps(f"mlp_ps{k}", [P, U]) for k in range(4)]

        ids_in = sem("ids_in")
        rows_made = sem("rows_made")
        idx_set = sem("idx_set")
        w0_in = sem("w0_in")
        w1_in = sem("w1_in")
        mlp_in = sem("mlp_in")
        w0_folded = sem("w0_folded")
        w1_rounded = sem("w1_rounded")
        w1_split = sem("w1_split")
        gathered = [sem(f"gathered{q}") for q in range(RU)]
        x_stored = [sem(f"x_stored{q}") for q in range(RU)]
        base_in = sem("base_in")
        shifted_in = [sem(f"shifted_in{n}") for n in range(len(PARTS0))]
        feat_in = [sem(f"feat_in{k}") for k in range(2)]
        hid_in = [sem(f"hid_in{k}") for k in range(2)]
        z0_made = sem("z0_made")
        zp_made = sem("zp_made")
        zs_made = sem("zs_made")
        hi_made = sem("hi_made")
        lo_made = sem("lo_made")
        cur0_done = sem("cur0_done")
        zp_used = sem("zp_used")
        split_used = sem("split_used")
        act0_done = sem("act0_done")
        act1_done = sem("act1_done")
        h_stored = [sem(f"h_stored{k}") for k in range(2)]
        sum0_done = sem("sum0_done")
        sum1_done = sem("sum1_done")
        mlp_mm = sem("mlp_mm")
        mlp_act = sem("mlp_act")
        y_stored = sem("y_stored")
        X_STORES = FB + 2

        block = ctx.enter_context(nc.Block())

        def rounds(engine, body):
            body(0, True, False)
            with engine.Fori(1, ROUNDS - 1) as r:
                body(r, False, False)
            body(ROUNDS - 1, False, True)

        @block.gpsimd
        def _(pool):
            def gather(q, indices):
                for g in range(FG):
                    nc.gpsimd.indirect_dma_start(
                        emb[q][:, g, :], None, table,
                        bass.IndirectOffsetOnAxis(indices[:, g:g + 1], 0)).then_inc(gathered[q], 16)

            pool.wait_ge(rows_made, 1)
            for q in range(RU):
                gather(q, rows_sb[:, q * FG:(q + 1) * FG])
            with pool.Fori(1, ROUNDS) as r:
                for q in range(RU):
                    pool.wait_ge(gathered[q], 16 * FG * r)
                    pool.wait_ge(x_stored[q], 16 * X_STORES * r)
                nc.gpsimd.tensor_copy(idx[:], rows_sb[:, bass.ts(r, RU * FG)]).then_inc(idx_set, 1)
                pool.wait_ge(rows_made, 1)
                pool.wait_ge(idx_set, r)
                for q in range(RU):
                    gather(q, idx[:, q * FG:(q + 1) * FG])

        @block.sync
        def _(sp):
            sp.dma_start(ids_sb[:], ids).then_inc(ids_in, 16)
            sp.dma_start(base_sb[:], id_base).then_inc(ids_in, 16)
            sp.dma_start(w0_sb[:], w0_ij).then_inc(w0_in, 16)
            sp.dma_start(w0_back, w0_ji).then_inc(w0_in, 16)
            sp.dma_start(w1_whole, w1[:, PLAIN:]).then_inc(w1_in, 16)
            sp.dma_start(w1_sb[:], w1[:, 0:PLAIN]).then_inc(w1_in, 16)

            def body(r, first, last, prologue=False):
                x_at = [(RU * r + k) * X_UNIT for k in range(RU + 3)]
                h_at = [(RU * r + k) * H_UNIT for k in range(RU + 1)]
                if not isinstance(r, int):
                    x_at = [sp.snap(x) for x in x_at]
                    h_at = [sp.snap(x) for x in h_at]

                def store_x(k):
                    q = k % RU
                    sp.wait_ge(gathered[q], 16 * FG * (r + k // RU) + 16 * FG)
                    for row, fb, g in [(FG * fb, fb, 0) for fb in range(FB)] + [(FIELDS + 1, 0, 1), (FIELDS + FG, 1, 0)]:
                        sp.dma_start(bass.AP(x_dram.tensor, x_at[k] + row * U, [[DIM, S], [U, FG - g], [1, DIM]]),
                                     emb[q][fb * S:(fb + 1) * S, g:, :]).then_inc(x_stored[q], 16)

                def load_pair(k, between=lambda: None):
                    if not (prologue and k == 0):
                        sp.wait_ge(z0_made, len(PARTS0) * (RU * r + k))
                    sp.wait_ge(x_stored[k % RU], 16 * X_STORES * (r + k // RU) + 16 * X_STORES)
                    sp.dma_start(base[:], bass.AP(x_dram.tensor, x_at[k], [
                        [U, FIELDS], [0, CYC], [1, U]])).then_inc(base_in, 16)
                    for n, (t0, t1) in enumerate(PARTS0):
                        if n == len(PARTS0) - 1:
                            between()
                        sp.dma_start(shifted[:, t0:t1, :], bass.AP(x_dram.tensor, x_at[k] + t0 * U, [
                            [U, FIELDS], [SHIFTS * U, CYC], [1, (t1 - t0) * U]])).then_inc(shifted_in[n], 16)

                def load_feat(k, free=True):
                    if free:
                        sp.wait_ge(zs_made, SPLIT * (RU * r + k) - SPLIT)
                    sp.dma_start(feat_rep[k % 2][:], bass.AP(x_dram.tensor, x_at[k], [
                        [0, GJ], [SI * U, GI], [1, SI * U]])).then_inc(feat_in[k % 2], 16)

                def store_hidden(k):
                    sp.wait_ge(act0_done, RU * r + k + 1)
                    sp.dma_start(bass.AP(h_dram.tensor, h_at[k], [[U, HALF], [1, U]]),
                                 act0[k % 2][HALF:, :]).then_inc(h_stored[k % 2], 16)

                def load_hidden(k):
                    sp.wait_ge(h_stored[k % 2], 16 * (RU // 2) * r + 16 * (k // 2) + 16)
                    sp.dma_start(hid_rep[k % 2][:], bass.AP(h_dram.tensor, h_at[k], [
                        [TJ * U, GJ], [0, GI], [1, TJ * U]])).then_inc(hid_in[k % 2], 16)

                if prologue:
                    store_x(0)
                    load_pair(0)
                    store_x(1)
                    load_feat(0, free=False)
                    load_pair(1, between=lambda: store_hidden(0))
                    load_hidden(0)
                    store_x(2)
                    return
                for q in range(RU):
                    if q + 1 < RU or not last:
                        load_feat(q + 1, free=not (first and q == 0))
                    if q + 2 < RU or not last:
                        load_pair(q + 2)
                    if q + 1 < RU or not last:
                        store_hidden(q + 1)
                        load_hidden(q + 1)
                    if q + 3 < RU or not last:
                        store_x(q + 3)

            body(0, True, False, prologue=True)
            sp.dma_start(wt1_sb[0:HALF, 0, :], w_top1[0:HALF, :]).then_inc(mlp_in, 16)
            sp.dma_start(wt1_sb[:, 1, :], w_top1[HALF:HALF + P, :]).then_inc(mlp_in, 16)
            sp.dma_start(wt1_sb[HALF:DIRECT_DENSE, 0, :], w_top1[HALF + P:, :]).then_inc(mlp_in, 16)
            sp.dma_start(wt2_sb[:], w_top2.rearrange("(k p) m -> p k m", p=P)).then_inc(mlp_in, 16)
            sp.dma_start(wt3_sb[:], w_top3).then_inc(mlp_in, 16)
            sp.dma_start(bt1_sb[:], b_top1).then_inc(mlp_in, 16)
            sp.dma_start(bt2_sb[:], b_top2).then_inc(mlp_in, 16)
            sp.dma_start(top0[HALF:DIRECT_DENSE, :], dense_t).then_inc(mlp_in, 16)
            rounds(sp, body)
            sp.wait_ge(mlp_act, GROUPS * ROUNDS)
            sp.dma_start(out.rearrange("b o -> o b"), y_sb[:]).then_inc(y_stored, 16)
            sp.wait_ge(y_stored, 16)
            for q in range(RU):
                sp.wait_ge(x_stored[q], 16 * X_STORES * ROUNDS)
            for k in range(2):
                sp.wait_ge(h_stored[k], 16 * UNITS // 2)

        @block.scalar
        def _(act):
            act.wait_ge(w1_in, 32)
            nc.scalar.activation(w1_hi[:], w1_whole, ACT.Copy).then_inc(w1_rounded, 1)

            def relu0(r, k, begin=False):
                act.wait_ge(cur0_done, RU * r + k + 1)
                if not begin:
                    act.wait_ge(h_stored[k % 2], 16 * (RU // 2) * r + 16 * (k // 2))
                    act.wait_ge(sum0_done, RU * r + k - 1)
                nc.scalar.activation(act0[k % 2][:], cur0[k % 2][:], ACT.Relu).then_inc(act0_done, 1)

            def relu1(r, k, begin=False):
                act.wait_ge(split_used, SPLIT * (RU * r + k) + SPLIT)
                if not begin:
                    act.wait_ge(sum1_done, RU * r + k)
                nc.scalar.activation(act1[:], cur1[k % 2][:], ACT.Relu).then_inc(act1_done, 1)

            def mlp1(n):
                for m in range(M1):
                    act.wait_ge(mlp_mm, n + m + 1)
                    nc.scalar.activation(h1[:, m, :], mlp_ps[m][:, 0:RS], ACT.Relu, bias=bt1_sb[:, m:m + 1]).then_inc(mlp_act, 1)

            def mlp2(n):
                for m in range(M2):
                    act.wait_ge(mlp_mm, n + m + 1)
                    nc.scalar.activation(h2[:, m, :], mlp_ps[m][:, 0:RS], ACT.Relu, bias=bt2_sb[:, m:m + 1]).then_inc(mlp_act, 1)

            def mlp3(r, n, bank=mlp_ps[M2]):
                act.wait_ge(mlp_mm, n + 1)
                nc.scalar.activation(y_sb[:, bass.ts(r, RS)], bank[0:1, 0:RS], ACT.Copy).then_inc(mlp_act, 1)

            def body(r, first, last):
                for q in range(RU):
                    begin = first and q == 0
                    if not begin:
                        relu1(r, q - 1, begin=first and q == 1)
                    if q + 1 < RU or not last:
                        relu0(r, q + 1, begin=begin)
                    for k in range(SPLIT):
                        act.wait_ge(zs_made, SPLIT * (RU * r + q) + k + 1)
                        if not begin:
                            act.wait_ge(split_used, SPLIT * (RU * r + q) - SPLIT + k + 1)
                        nc.scalar.activation(z_hi[k][:], zs[k][:], ACT.Copy).then_inc(hi_made, 1)
                    if not first:
                        if q == 1:
                            act.wait_ge(mlp_in, 16 * 8)
                            mlp1(GROUPS * (r - 1))
                        elif q == 2 and not last:
                            mlp2(GROUPS * (r - 1) + M1)
                        elif q == 3 and not last:
                            mlp3(r - 1, GROUPS * (r - 1) + M1 + M2)

            relu0(0, 0, begin=True)
            rounds(act, body)
            relu1(ROUNDS - 1, RU - 1)
            n = GROUPS * (ROUNDS - 2)
            mlp2(n + M1)
            mlp1(n + M1 + M2)
            mlp3(ROUNDS - 2, n + 2 * M1 + M2, bank=cur0[0])
            mlp2(n + 2 * M1 + M2 + 1)
            mlp3(ROUNDS - 1, n + 2 * M1 + 2 * M2 + 1)

        @block.vector
        def _(dve):
            dve.wait_ge(ids_in, 32)
            nc.vector.tensor_tensor(rows_sb[:].rearrange("p (u g) -> p u g", g=FG), ids_sb[:].rearrange("p (u g) -> p u g", g=FG),
                                    base_sb[:].unsqueeze(1).broadcast_to([P, UNITS, FG]), ALU.add).then_inc(rows_made, 1)
            dve.wait_ge(w0_in, 32)
            nc.vector.tensor_tensor(w0_sb[:], w0_sb[:], w0_back, ALU.add).then_inc(w0_folded, 1)
            dve.wait_ge(w1_rounded, 1)
            nc.vector.tensor_tensor(w1_lo[:], w1_whole, w1_hi[:].bitcast(f32), ALU.subtract).then_inc(w1_split, 1)

            def make_z0(r, k, begin=False):
                dve.wait_ge(base_in, 16 * (RU * r + k) + 16)
                if begin:
                    dve.wait_ge(w0_folded, 1)
                else:
                    dve.wait_ge(cur0_done, RU * r + k)
                for n, (t0, t1) in enumerate(PARTS0):
                    dve.wait_ge(shifted_in[n], 16 * (RU * r + k) + 16)
                    nc.vector.tensor_tensor(z0[:, t0:t1, :], shifted[:, t0:t1, :],
                                            base[:].unsqueeze(1).broadcast_to([PAIR0, t1 - t0, U]), ALU.mult).then_inc(z0_made, 1)

            def product(out_, q, t):
                hid = hid_rep[q % 2][:, t, :].unsqueeze(1).broadcast_to([P, SI, U])
                return nc.vector.tensor_tensor(out_, feat_rep[q % 2][:], hid, ALU.mult)

            def samples(r, k):
                return bass.ds((RU * r + k) * S, S)

            def sum0(r, k):
                dve.wait_ge(act0_done, RU * r + k + 1)
                nc.vector.tensor_reduce(top0[0:HALF, samples(r, k)], act0[k % 2][0:HALF, :].rearrange("p (s d) -> p s d", d=DIM), AX.X, ALU.add).then_inc(sum0_done, 1)

            def sum1(r, k):
                dve.wait_ge(act1_done, RU * r + k + 1)
                nc.vector.tensor_reduce(top1[:, samples(r, k)], act1[:].rearrange("p (s d) -> p s d", d=DIM), AX.X, ALU.add).then_inc(sum1_done, 1)

            make_z0(0, 0, begin=True)
            sum0(0, 0)

            def body(r, first, last):
                for q in range(RU):
                    begin = first and q == 0
                    unit = RU * r + q
                    if q + 1 < RU or not last:
                        make_z0(r, q + 1)
                    dve.wait_ge(feat_in[q % 2], 16 * (RU // 2) * r + 16 * (q // 2) + 16)
                    dve.wait_ge(hid_in[q % 2], 16 * (RU // 2) * r + 16 * (q // 2) + 16)
                    for t in range(PLAIN):
                        if not begin:
                            dve.wait_ge(zp_used, PLAIN * (unit - 1) + t + 1)
                        product(zp[t][:], q, t).then_inc(zp_made, 1)
                    for k in range(SPLIT):
                        if not begin:
                            dve.wait_ge(lo_made, SPLIT * unit - SPLIT + k + 1)
                        elif k == 0:
                            dve.wait_ge(w1_split, 1)
                        product(zs[k][:], q, PLAIN + k).then_inc(zs_made, 1)
                    if not begin:
                        sum1(r, q - 1)
                    for k in range(SPLIT):
                        dve.wait_ge(hi_made, SPLIT * unit + k + 1)
                        if not begin:
                            dve.wait_ge(split_used, SPLIT * unit - SPLIT + k + 1)
                        nc.vector.tensor_tensor(z_lo[k][:], zs[k][:], z_hi[k][:].bitcast(f32), ALU.subtract).then_inc(lo_made, 1)
                    if q + 1 < RU or not last:
                        sum0(r, q + 1)
            rounds(dve, body)
            sum1(ROUNDS - 1, RU - 1)

        @block.tensor
        def _(pe):
            def layer0(r, k, begin=False):
                if not begin:
                    pe.wait_ge(act0_done, RU * r + k - 1)
                for n, (t0, t1) in enumerate(PARTS0):
                    pe.wait_ge(z0_made, len(PARTS0) * (RU * r + k) + n + 1)
                    for t in range(t0, t1):
                        last = nc.tensor.matmul(cur0[k % 2][:], w0_sb[:, t, :], z0[:, t, :],
                                                start=t == 0, stop=t == SHIFTS - 1)
                last.then_inc(cur0_done, 1)

            def layer1(r, q, begin):
                bank = cur1[q % 2]
                unit = RU * r + q
                for t in range(PLAIN):
                    pe.wait_ge(zp_made, PLAIN * unit + t + 1)
                    if t == 0 and not begin:
                        pe.wait_ge(act1_done, unit - 1)
                    for s in range(SI):
                        last = nc.tensor.matmul(bank[:], w1_sb[:, t, s, :], zp[t][:, s, :],
                                                start=t == 0 and s == 0, stop=False)
                    last.then_inc(zp_used, 1)
                for k in range(SPLIT):
                    pe.wait_ge(hi_made, SPLIT * unit + k + 1)
                    for s in range(SI):
                        nc.tensor.matmul(bank[:], w1_hi[:, k, s, :], z_hi[k][:, s, :], start=False, stop=False)
                        nc.tensor.matmul(bank[:], w1_lo[:, k, s, :], z_hi[k][:, s, :], start=False, stop=False)
                    pe.wait_ge(lo_made, SPLIT * unit + k + 1)
                    for s in range(SI):
                        end = k == SPLIT - 1 and s == SI - 1
                        last = nc.tensor.matmul(bank[:], w1_hi[:, k, s, :], z_lo[k][:, s, :], start=False, stop=end)
                    last.then_inc(split_used, 1)

            def mlp1(r, begin=False):
                pe.wait_ge(mlp_in, 16 * 8)
                pe.wait_ge(sum0_done, RU * r + RU)
                pe.wait_ge(sum1_done, RU * r + RU)
                for m in range(M1):
                    for part, src in enumerate((top0, top1)):
                        last = nc.tensor.matmul(mlp_ps[m][:, 0:RS], wt1_sb[0:src.shape[0], part, m * P:(m + 1) * P],
                                                src[:, bass.ts(r, RS)], start=part == 0, stop=part == 1)
                    last.then_inc(mlp_mm, 1)

            def mlp2(n):
                pe.wait_ge(mlp_act, n)
                for m in range(M2):
                    for k in range(M1):
                        last = nc.tensor.matmul(mlp_ps[m][:, 0:RS], wt2_sb[:, k, m * P:(m + 1) * P], h1[:, k, :],
                                                start=k == 0, stop=k == M1 - 1)
                    last.then_inc(mlp_mm, 1)

            def mlp3(n, bank=mlp_ps[M2]):
                pe.wait_ge(mlp_act, n)
                for k in range(M2):
                    last = nc.tensor.matmul(bank[0:1, 0:RS], wt3_sb[:, k:k + 1], h2[:, k, :],
                                            start=k == 0, stop=k == M2 - 1)
                last.then_inc(mlp_mm, 1)

            def body(r, first, last):
                for q in range(RU):
                    if q + 1 < RU or not last:
                        layer0(r, q + 1, begin=first and q == 0)
                    if not first:
                        if q == 1:
                            mlp1(r - 1)
                        elif q == 2 and not last:
                            mlp2(GROUPS * (r - 1) + M1)
                        elif q == 3 and not last:
                            mlp3(GROUPS * (r - 1) + M1 + M2)
                    layer1(r, q, first and q < 2)
                if not first and not last:
                    pe.wait_ge(mlp_act, GROUPS * r)

            pe.wait_ge(w0_folded, 1)
            pe.wait_ge(x_stored[0], 16 * X_STORES)
            for _ in range(8):
                nc.tensor.matmul(mlp_ps[3][:], w0_sb[:, 0, :], w0_sb[:, 0:U // WIDE, :], start=True, stop=True)
            layer0(0, 0, begin=True)
            pe.wait_ge(w1_split, 1)
            rounds(pe, body)
            n = GROUPS * (ROUNDS - 2)
            mlp2(n + M1)
            pe.wait_ge(mlp_act, n + M1 + M2)
            mlp1(ROUNDS - 1)
            pe.wait_ge(act0_done, UNITS)
            mlp3(n + M1 + M2, bank=cur0[0])
            mlp2(n + 2 * M1 + M2)
            mlp3(n + 2 * M1 + 2 * M2 + 1)


def pair_rows():
    ij = np.full((FIELDS, CYC, SHIFTS), -1)
    ji = ij.copy()
    for i in range(FIELDS):
        for c in range(CYC):
            for t in range(SHIFTS):
                far = SHIFTS * c + t
                j = (i + far) % FIELDS
                if far <= FIELDS // 2:
                    ij[i, c, t] = i * FIELDS + j
                    if far:
                        ji[i, c, t] = j * FIELDS + i
    return ij.reshape(PAIR0, SHIFTS), ji.reshape(PAIR0, SHIFTS)


def kernel(**inputs):
    import concourse.bacc as bacc
    from concourse.bass_utils import run_bass_kernel_spmd

    a = {k: np.asarray(v) for k, v in inputs.items()}
    tables = [a[f"tbl_{f}"] for f in range(FIELDS)]
    begin = np.cumsum([0] + [t.shape[0] for t in tables])[:FIELDS].astype(np.int32)
    fields = np.append(np.arange(FIELDS), 0)
    ids = a["ids"][:, fields].reshape(UNITS, S, FB, FG).transpose(2, 1, 0, 3).reshape(P, UNITS * FG)
    id_base = np.repeat(begin[fields].reshape(FB, FG), S, axis=0)
    w0 = a["L0_rec_W0"]
    w0 = np.concatenate([np.concatenate([w0[:, HALF:], w0[:, :HALF]], 1), np.zeros((1, WIDE), w0.dtype)])
    ij, ji = pair_rows()
    w1 = a["L0_rec_W1"].reshape(FIELDS, HALF, WIDE)
    w1 = np.concatenate([w1, np.zeros((GI * SI - FIELDS, HALF, WIDE), w1.dtype)])
    w1 = w1.reshape(GI, SI, GJ, TJ, WIDE).transpose(2, 0, 3, 1, 4).reshape(P, TJ, SI, WIDE)
    arrays = {
        "table": np.concatenate(tables), "ids": ids, "id_base": id_base,
        "w0_ij": w0[ij], "w0_ji": w0[ji], "w1": w1, "dense_t": a["dense_ctx"].T,
        "w_top1": a["W_top1"], "w_top2": a["W_top2"],
        "b_top1": a["b_top1"].reshape(-1, P).T, "b_top2": a["b_top2"].reshape(-1, P).T,
        "w_top3": a["W_top3"].reshape(-1, P).T,
    }
    arrays = {k: np.ascontiguousarray(v) for k, v in arrays.items()}

    nc = bacc.Bacc("TRN2", target_bir_lowering=False, num_devices=1)
    aps = {k: nc.dram_tensor(k, v.shape, mybir.dt.from_np(v.dtype), kind="ExternalInput").ap() for k, v in arrays.items()}
    out = nc.dram_tensor("out", (BATCH, 1), mybir.dt.float32, kind="ExternalOutput").ap()
    tower(nc, out=out, **aps)
    r = run_bass_kernel_spmd(nc, [arrays], core_ids=[0])
    return r.results[0]["out"]
```
